# Optimizing a Trainium2 kernel written in Bass

```python
import numpy as np
import jax
import jax.numpy as jnp

def _softmax(x, axis=-1):
    return jax.nn.softmax(x, axis=axis)

def _gelu(x):
    return jax.nn.gelu(x, approximate=True)

def _silu(x):
    return jax.nn.silu(x)

def _sigmoid(x):
    return jax.nn.sigmoid(x)

def _layernorm(x, axis=-1, eps=1e-05):
    m = jnp.mean(x, axis=axis, keepdims=True)
    v = jnp.var(x, axis=axis, keepdims=True)
    return (x - m) / jnp.sqrt(v + eps)

def _scatter_add(tgt, idx, src, axis=0):
    return tgt.at[idx].add(src)

def _segment_sum(src, seg, n):
    return jax.ops.segment_sum(src, seg, n)
kernel_name = 'mk_xattn_seq_d2_seqx_r2_007d8a'

def setup_inputs(seed: int=0):
    np.random.seed(seed)
    _w = jnp.asarray

    def _rec_inputs():
        import jax
        import jax.numpy as jnp
        _rk = jax.random.key(seed)
        x = 7.22e-05 + 1 * jax.random.normal(jax.random.fold_in(_rk, 1), (16, 256, 2048), jnp.float32)
        _lenS = 256 - jax.random.randint(jax.random.fold_in(_rk, 7), (16,), 0, max(1, 256 // 4) + 1, jnp.int32)
        _lenS2 = 256 - jax.random.randint(jax.random.fold_in(_rk, 8), (16,), 0, max(1, 256 // 4) + 1, jnp.int32)
        _ctx_4096P = jax.random.normal(jax.random.fold_in(_rk, 11), (16, 16, 2048), jnp.float32)
        _ctx_4096c = jax.random.dirichlet(jax.random.fold_in(_rk, 511), 0.3 * jnp.ones((16,), jnp.float32), (16, 256))
        _ctx_4096t = jnp.einsum('bsk,bkd->bsd', _ctx_4096c, _ctx_4096P)
        _ctx_4096t = _ctx_4096t * jax.lax.rsqrt(jnp.mean(jnp.square(_ctx_4096t)) + 1e-12) * 0.953939
        ctx_4096 = 4.13588e-05 + 0.999923 * (_ctx_4096t + 0.3 * jax.random.normal(jax.random.fold_in(_rk, 611), (16, 256, 2048), jnp.float32))
        _validS = jnp.arange(256)[None, :] < _lenS[:, None]
        _validS2 = jnp.arange(256)[None, :] < _lenS2[:, None]
        _causal = jnp.tril(jnp.ones((256, 256), dtype=bool))
        mask_Bx1x4096_ff1 = jnp.where(jnp.ones((16, 1, 2048), dtype=bool), 1.0, 0.0).astype(jnp.float32)
        return (x, ctx_4096, mask_Bx1x4096_ff1)
    x, ctx_4096, mask_Bx1x4096_ff1 = _rec_inputs()

    def _L0_xattn_setup():
        import jax, jax.numpy as jnp
        import numpy as np
        NUM_HEADS = 8
        CHUNK = 64
        EPS = 1e-05
        NEG = -1000000000.0

        def _chunk_attn(q, k, v, masks, W_in, b_in, W_out, b_out):
            N, C, T = q.shape
            H, Dh = (NUM_HEADS, C // NUM_HEADS)
            nc = T // CHUNK
            Wq, Wk, Wv = jnp.split(W_in, 3, axis=0)
            bq, bk, bv = jnp.split(b_in, 3, axis=0)

            def proj(t, W, b):
                t = t.transpose(0, 2, 1) @ W.T + b
                return t.reshape(N, nc, CHUNK, H, Dh)
            qh = proj(q, Wq, bq)
            kh = proj(k, Wk, bk)
            vh = proj(v, Wv, bv)
            scale = 1.0 / jnp.sqrt(jnp.asarray(Dh, q.dtype))
            scores = jnp.einsum('bnqhd,bnkhd->bnhqk', qh, kh) * scale
            km = masks[:, 0, :].reshape(N, nc, CHUNK)
            scores = scores + jnp.where(km[:, :, None, None, :] > 0, 0.0, NEG)
            attn = jax.nn.softmax(scores, axis=-1)
            out = jnp.einsum('bnhqk,bnkhd->bnqhd', attn, vh).reshape(N, T, C)
            out = out @ W_out.T + b_out
            out = out.transpose(0, 2, 1) * masks
            return out
        key = jax.random.key(seed)
        ks = jax.random.split(key, 8)
        N, C, T = (4, 256, 2048)
        x = jax.random.normal(ks[0], (N, C, T), dtype=jnp.float32)
        q = jax.random.normal(ks[1], (N, C, T), dtype=jnp.float32)
        k = jax.random.normal(ks[2], (N, C, T), dtype=jnp.float32)
        v = jax.random.normal(ks[3], (N, C, T), dtype=jnp.float32)
        masks = jnp.ones((N, 1, T), dtype=jnp.float32)
        s = 1.0 / np.sqrt(C)
        W_in = jax.random.normal(ks[4], (3 * C, C), dtype=jnp.float32) * s
        b_in = jnp.zeros((3 * C,), dtype=jnp.float32)
        W_out = jax.random.normal(ks[5], (C, C), dtype=jnp.float32) * s
        b_out = jnp.zeros((C,), dtype=jnp.float32)
        return {'x': x, 'q': q, 'k': k, 'v': v, 'masks': masks, 'W_in': W_in, 'b_in': b_in, 'W_out': W_out, 'b_out': b_out}
    _L0_xattn_all = _L0_xattn_setup()
    _L0_xattn_in = {k: v for k, v in _L0_xattn_all.items() if k in ('W_in', 'b_in', 'W_out', 'b_out')}
    del _L0_xattn_all

    def _L1_xattn_setup():
        import jax, jax.numpy as jnp
        import numpy as np
        NUM_HEADS = 8
        CHUNK = 64
        EPS = 1e-05
        NEG = -1000000000.0

        def _chunk_attn(q, k, v, masks, W_in, b_in, W_out, b_out):
            N, C, T = q.shape
            H, Dh = (NUM_HEADS, C // NUM_HEADS)
            nc = T // CHUNK
            Wq, Wk, Wv = jnp.split(W_in, 3, axis=0)
            bq, bk, bv = jnp.split(b_in, 3, axis=0)

            def proj(t, W, b):
                t = t.transpose(0, 2, 1) @ W.T + b
                return t.reshape(N, nc, CHUNK, H, Dh)
            qh = proj(q, Wq, bq)
            kh = proj(k, Wk, bk)
            vh = proj(v, Wv, bv)
            scale = 1.0 / jnp.sqrt(jnp.asarray(Dh, q.dtype))
            scores = jnp.einsum('bnqhd,bnkhd->bnhqk', qh, kh) * scale
            km = masks[:, 0, :].reshape(N, nc, CHUNK)
            scores = scores + jnp.where(km[:, :, None, None, :] > 0, 0.0, NEG)
            attn = jax.nn.softmax(scores, axis=-1)
            out = jnp.einsum('bnhqk,bnkhd->bnqhd', attn, vh).reshape(N, T, C)
            out = out @ W_out.T + b_out
            out = out.transpose(0, 2, 1) * masks
            return out
        key = jax.random.key(seed)
        ks = jax.random.split(key, 8)
        N, C, T = (4, 256, 2048)
        x = jax.random.normal(ks[0], (N, C, T), dtype=jnp.float32)
        q = jax.random.normal(ks[1], (N, C, T), dtype=jnp.float32)
        k = jax.random.normal(ks[2], (N, C, T), dtype=jnp.float32)
        v = jax.random.normal(ks[3], (N, C, T), dtype=jnp.float32)
        masks = jnp.ones((N, 1, T), dtype=jnp.float32)
        s = 1.0 / np.sqrt(C)
        W_in = jax.random.normal(ks[4], (3 * C, C), dtype=jnp.float32) * s
        b_in = jnp.zeros((3 * C,), dtype=jnp.float32)
        W_out = jax.random.normal(ks[5], (C, C), dtype=jnp.float32) * s
        b_out = jnp.zeros((C,), dtype=jnp.float32)
        return {'x': x, 'q': q, 'k': k, 'v': v, 'masks': masks, 'W_in': W_in, 'b_in': b_in, 'W_out': W_out, 'b_out': b_out}
    _L1_xattn_all = _L1_xattn_setup()
    _L1_xattn_in = {k: v for k, v in _L1_xattn_all.items() if k in ('W_in', 'b_in', 'W_out', 'b_out')}
    del _L1_xattn_all
    return {'x': x, 'ctx_4096': ctx_4096, 'mask_Bx1x4096_ff1': mask_Bx1x4096_ff1, 'L0_xattn_W_in': _L0_xattn_in['W_in'], 'L0_xattn_b_in': _L0_xattn_in['b_in'], 'L0_xattn_W_out': _L0_xattn_in['W_out'], 'L0_xattn_b_out': _L0_xattn_in['b_out'], 'L1_xattn_W_in': _L1_xattn_in['W_in'], 'L1_xattn_b_in': _L1_xattn_in['b_in'], 'L1_xattn_W_out': _L1_xattn_in['W_out'], 'L1_xattn_b_out': _L1_xattn_in['b_out']}

def reference(x, ctx_4096, mask_Bx1x4096_ff1, L0_xattn_W_in, L0_xattn_b_in, L0_xattn_W_out, L0_xattn_b_out, L1_xattn_W_in, L1_xattn_b_in, L1_xattn_W_out, L1_xattn_b_out):
    import jax
    import jax.numpy as jnp

    def _L0_xattn_ref(x, q, k, v, masks, W_in, b_in, W_out, b_out):
        import jax, jax.numpy as jnp
        import numpy as np
        NUM_HEADS = 8
        CHUNK = 64
        EPS = 1e-05
        NEG = -1000000000.0

        def _chunk_attn(q, k, v, masks, W_in, b_in, W_out, b_out):
            N, C, T = q.shape
            H, Dh = (NUM_HEADS, C // NUM_HEADS)
            nc = T // CHUNK
            Wq, Wk, Wv = jnp.split(W_in, 3, axis=0)
            bq, bk, bv = jnp.split(b_in, 3, axis=0)

            def proj(t, W, b):
                t = t.transpose(0, 2, 1) @ W.T + b
                return t.reshape(N, nc, CHUNK, H, Dh)
            qh = proj(q, Wq, bq)
            kh = proj(k, Wk, bk)
            vh = proj(v, Wv, bv)
            scale = 1.0 / jnp.sqrt(jnp.asarray(Dh, q.dtype))
            scores = jnp.einsum('bnqhd,bnkhd->bnhqk', qh, kh) * scale
            km = masks[:, 0, :].reshape(N, nc, CHUNK)
            scores = scores + jnp.where(km[:, :, None, None, :] > 0, 0.0, NEG)
            attn = jax.nn.softmax(scores, axis=-1)
            out = jnp.einsum('bnhqk,bnkhd->bnqhd', attn, vh).reshape(N, T, C)
            out = out @ W_out.T + b_out
            out = out.transpose(0, 2, 1) * masks
            return out
        out = _chunk_attn(q, k, v, masks, W_in, b_in, W_out, b_out) + x
        mu = jnp.mean(out, axis=2, keepdims=True)
        var = jnp.mean(jnp.square(out - mu), axis=2, keepdims=True)
        return (out - mu) * jax.lax.rsqrt(var + EPS)

    def _L1_xattn_ref(x, q, k, v, masks, W_in, b_in, W_out, b_out):
        import jax, jax.numpy as jnp
        import numpy as np
        NUM_HEADS = 8
        CHUNK = 64
        EPS = 1e-05
        NEG = -1000000000.0

        def _chunk_attn(q, k, v, masks, W_in, b_in, W_out, b_out):
            N, C, T = q.shape
            H, Dh = (NUM_HEADS, C // NUM_HEADS)
            nc = T // CHUNK
            Wq, Wk, Wv = jnp.split(W_in, 3, axis=0)
            bq, bk, bv = jnp.split(b_in, 3, axis=0)

            def proj(t, W, b):
                t = t.transpose(0, 2, 1) @ W.T + b
                return t.reshape(N, nc, CHUNK, H, Dh)
            qh = proj(q, Wq, bq)
            kh = proj(k, Wk, bk)
            vh = proj(v, Wv, bv)
            scale = 1.0 / jnp.sqrt(jnp.asarray(Dh, q.dtype))
            scores = jnp.einsum('bnqhd,bnkhd->bnhqk', qh, kh) * scale
            km = masks[:, 0, :].reshape(N, nc, CHUNK)
            scores = scores + jnp.where(km[:, :, None, None, :] > 0, 0.0, NEG)
            attn = jax.nn.softmax(scores, axis=-1)
            out = jnp.einsum('bnhqk,bnkhd->bnqhd', attn, vh).reshape(N, T, C)
            out = out @ W_out.T + b_out
            out = out.transpose(0, 2, 1) * masks
            return out
        out = _chunk_attn(q, k, v, masks, W_in, b_in, W_out, b_out) + x
        mu = jnp.mean(out, axis=2, keepdims=True)
        var = jnp.mean(jnp.square(out - mu), axis=2, keepdims=True)
        return (out - mu) * jax.lax.rsqrt(var + EPS)
    x = _L0_xattn_ref(x, ctx_4096, ctx_4096, ctx_4096, mask_Bx1x4096_ff1, L0_xattn_W_in, L0_xattn_b_in, L0_xattn_W_out, L0_xattn_b_out)
    x = _L1_xattn_ref(x, ctx_4096, ctx_4096, ctx_4096, mask_Bx1x4096_ff1, L1_xattn_W_in, L1_xattn_b_in, L1_xattn_W_out, L1_xattn_b_out)
    return x

_drawn_inputs = setup_inputs


def setup_inputs(seed=0):
    import zlib

    import numpy as np

    out = dict(_drawn_inputs(seed))
    spreads = {'L0_xattn_b_in': (0.0, 0.552),
     'L0_xattn_b_out': (0.0, 0.8),
     'L1_xattn_b_in': (0.0, 0.509),
     'L1_xattn_b_out': (0.0, 0.8)}
    factors = {}
    for name, (base, spread) in spreads.items():
        noise = np.random.default_rng([zlib.crc32(name.encode()), seed]).standard_normal(out[name].shape)
        drawn = base * np.exp(spread * noise) if base else spread * noise
        out[name] = jnp.asarray(drawn.astype(out[name].dtype))
    for name, factor in factors.items():
        out[name] = (out[name] * factor).astype(out[name].dtype)
    return out
```

```python
import concourse.bass as bass
from concourse import mybir
from contextlib import ExitStack

BATCH, CH, TIME = 16, 256, 2048
HEADS, CHUNK = 8, 64
HEAD_DIM = CH // HEADS
LAYERS = 2
P = 128
KT = CH // P
BLK = 512
PAIRS = BLK // (2 * CHUNK)
CHUNKS = BLK // CHUNK
BLOCKS_PER_BATCH = TIME // BLK
BLOCKS = BATCH * BLOCKS_PER_BATCH
UNITS = BLOCKS * LAYERS
STEPS = UNITS * PAIRS
HEADS_PER_TILE = P // HEAD_DIM
SCALE = float(HEAD_DIM) ** -0.5
NEG = -1.0e9
EPS = 1.0e-5
SOFT = 4
RES_RING = 8
ATT_RING = 4


def build_attention(nc, x, ctx_in, mask, w_in_t, b_in, w_out_t, b_out, out):
    f32, f32r = mybir.dt.float32, mybir.dt.float32r
    ALU, ACT, AX = mybir.AluOpType, mybir.ActivationFunctionType, mybir.AxisListType

    ctx_blocks = ctx_in.rearrange("n (k p) (b t) -> n b p k t", p=P, t=BLK)
    x_blocks = x.rearrange("n (k p) (b t) -> n b p k t", p=P, t=BLK)
    out_blocks = out.rearrange("n (k p) (b t) -> n b p k t", p=P, t=BLK)
    mask_rows = mask.rearrange("n o (b t) -> n b (o t)", t=BLK)
    mask_keys = mask.rearrange("n o (b p c k) -> n b c (o p) k", p=PAIRS, c=2, k=CHUNK)

    with ExitStack() as es:
        def sb(name, shape, dt=f32):
            return es.enter_context(nc.sbuf_tensor(name, shape, dt))

        def pb(name):
            return es.enter_context(nc.psum_tensor(name, [P, 512], f32))

        def sem(name):
            return es.enter_context(nc.semaphore(name))

        w_in_hi = [sb(f"w_in_hi{l}", [P, KT, 3 * CH], f32r) for l in range(LAYERS)]
        w_in_lo = [sb(f"w_in_lo{l}", [P, KT, 3 * CH], f32r) for l in range(LAYERS)]
        w_out_hi = [sb(f"w_out_hi{l}", [P, KT, CH], f32r) for l in range(LAYERS)]
        w_out_lo = [sb(f"w_out_lo{l}", [P, KT, CH], f32r) for l in range(LAYERS)]
        bias_in = sb("bias_in", [P, LAYERS, 3 * KT])
        bias_q = sb("bias_q", [P, LAYERS, KT])
        bias_out = sb("bias_out", [P, LAYERS, KT])
        ident = sb("ident", [P, P])
        ctx_raw = sb("ctx_raw", [P, KT, BLK])
        ctx_hi = sb("ctx_hi", [P, KT, BLK], f32r)
        ctx_lo = sb("ctx_lo", [P, KT, BLK], f32r)
        x_raw = sb("x_raw", [P, KT, BLK])
        q_sb = [sb(f"q{l}", [P, KT, BLK]) for l in range(LAYERS)]
        k_sb = [sb(f"k{l}", [P, KT, CHUNKS, HEADS_PER_TILE, CHUNK]) for l in range(LAYERS)]
        v_sb = [sb(f"v{l}", [P, PAIRS, 2, CH // 2]) for l in range(LAYERS)]
        soft = [sb(f"soft{j}", [P, HEADS, CHUNK]) for j in range(SOFT)]
        softT = [sb(f"softT{j}", [P, HEADS // 2, P]) for j in range(2)]
        top = sb("top", [P, SOFT, HEADS])
        total = sb("total", [P, SOFT, HEADS])
        inv_total = sb("inv_total", [P, SOFT, HEADS])
        o_hi = sb("o_hi", [P, KT, BLK], f32r)
        o_lo = sb("o_lo", [P, KT, BLK], f32r)
        mask0 = sb("mask0", [P, BLK])
        mask1 = sb("mask1", [P, BLK])
        mask_bc = [mask0, mask1]
        key_mask = sb("key_mask", [P, PAIRS, CHUNK])
        key_neg = sb("key_neg", [P, PAIRS, CHUNK])
        masked_out = sb("masked_out", [P, KT, BLK])
        res = sb("res", [P, RES_RING, KT, BLK])
        att1 = sb("att1", [P, ATT_RING, KT, BLK])
        stats = [sb(f"stats{l}", [P, KT, BLOCKS_PER_BATCH, 6]) for l in range(LAYERS)]
        mean_var = [sb(f"mean_var{l}", [P, KT, 2]) for l in range(LAYERS)]
        var_eps = sb("var_eps", [P, LAYERS, KT])
        rstd = sb("rstd", [P, LAYERS, KT])
        minus_half = sb("minus_half", [P, LAYERS, KT])

        scores = [pb("scores0"), pb("scores1")]
        proj = [pb("proj0"), pb("proj1")]
        probsT = [pb("probsT0"), pb("probsT1")]
        att = [pb("att0"), pb("att1_ps")]

        stage = res[:, :, :, :].rearrange("p a k t -> p (a k t)")
        PER_LAYER = KT * 3 * CH + KT * CH
        w_in_raw = [stage[:, l * PER_LAYER:l * PER_LAYER + KT * 3 * CH].rearrange("p (k n) -> p k n", k=KT)
                    for l in range(LAYERS)]
        w_out_raw = [stage[:, l * PER_LAYER + KT * 3 * CH:(l + 1) * PER_LAYER].rearrange("p (k n) -> p k n", k=KT)
                     for l in range(LAYERS)]

        w_loaded, bias_loaded = sem("w_loaded"), sem("bias_loaded")
        ctx_loaded, x_loaded, keymask_loaded = sem("ctx_loaded"), sem("x_loaded"), sem("keymask_loaded")
        mask_loaded = [sem("mask0_loaded"), sem("mask1_loaded")]
        out_stored = sem("out_stored")
        keys_zeroed, ident_ready, consts_ready = sem("keys_zeroed"), sem("ident_ready"), sem("consts_ready")
        w_hi_ready, w_lo_ready, bias_q_ready = sem("w_hi_ready"), sem("w_lo_ready"), sem("bias_q_ready")
        q_filled, k_filled, v_filled, w_filled = sem("q_filled"), sem("k_filled"), sem("v_filled"), sem("w_filled")
        scores_filled, probsT_filled, att_filled = sem("scores_filled"), sem("probsT_filled"), sem("att_filled")
        q_stored, k_stored, v_stored, o_hi_stored = sem("q_stored"), sem("k_stored"), sem("v_stored"), sem("o_hi_stored")
        ctx_hi_ready, exp_done, softT_stored = sem("ctx_hi_ready"), sem("exp_done"), sem("softT_stored")
        masked, topped, shifted = sem("masked"), sem("topped"), sem("shifted")
        totalled, inverted = sem("totalled"), sem("inverted")
        o_lo_stored, w_taken, ctx_lo_ready = sem("o_lo_stored"), sem("w_taken"), sem("ctx_lo_ready")
        key_neg_ready, res_added = sem("key_neg_ready"), sem("res_added")
        stats_done, aggregated, var_ready = sem("stats_done"), sem("aggregated"), sem("var_ready")
        norm0_done, norm1_done = sem("norm0_done"), sem("norm1_done")
        divided, res1_added, rstd_ready = sem("divided"), sem("res1_added"), sem("rstd_ready")

        pe_waited, dve_waited = sem("pe_waited"), sem("dve_waited")

        block = es.enter_context(nc.Block())

        def reached(eng, semaphore, count):
            if not (isinstance(count, int) and count <= 0):
                eng.wait_ge(semaphore, count)

        @block.sync
        def _(sp):
            def load_ctx(i):
                sp.dma_start(ctx_raw[:], ctx_blocks[i // BLOCKS_PER_BATCH, i % BLOCKS_PER_BATCH])\
                  .then_inc(ctx_loaded, 16)

            def load_key_mask(i):
                for c in range(2):
                    src = mask_keys[i // BLOCKS_PER_BATCH, i % BLOCKS_PER_BATCH, c]
                    sp.dma_start(key_mask[c * CHUNK:(c + 1) * CHUNK], src.partition_broadcast(CHUNK))\
                      .then_inc(keymask_loaded, 16)

            def load_mask(l, i):
                src = mask_rows[i // BLOCKS_PER_BATCH, i % BLOCKS_PER_BATCH]
                sp.dma_start(mask_bc[l][:], src.partition_broadcast(P)).then_inc(mask_loaded[l], 16)

            def store_out(i):
                sp.wait_ge(norm1_done, i + 1)
                sp.dma_start(out_blocks[i // BLOCKS_PER_BATCH, i % BLOCKS_PER_BATCH], res[:, i % RES_RING])\
                  .then_inc(out_stored, 16)

            def sp_block(i, has_ctx=True, has_next=True, has_out=False, first=False):
                reached(sp, res_added, 2 * i)
                sp.dma_start(x_raw[:], x_blocks[i // BLOCKS_PER_BATCH, i % BLOCKS_PER_BATCH]).then_inc(x_loaded, 16)
                reached(sp, w_taken, 4 * i - 2)
                if not first:
                    load_mask(1, i - 1)
                load_mask(0, i)
                if has_next:
                    sp.wait_ge(key_neg_ready, i + 1)
                    load_key_mask(i + 1)
                if has_out:
                    store_out(i - RES_RING)
                if has_ctx:
                    sp.wait_ge(ctx_lo_ready, i + 2)
                    load_ctx(i + 2)

            load_ctx(0)
            for l in range(LAYERS):
                sp.dma_start(w_in_raw[l], w_in_t[l].rearrange("(k p) n -> p k n", p=P)).then_inc(w_loaded, 16)
                sp.dma_start(w_out_raw[l], w_out_t[l].rearrange("(k p) n -> p k n", p=P)).then_inc(w_loaded, 16)
                sp.dma_start(bias_in[:, l], b_in[l]).then_inc(bias_loaded, 16)
                sp.dma_start(bias_out[:, l], b_out[l]).then_inc(bias_loaded, 16)
            load_key_mask(0)
            sp.wait_ge(ctx_lo_ready, 1)
            load_ctx(1)
            sp_block(0, first=True)
            with sp.Fori(1, RES_RING) as i:
                sp_block(i)
            with sp.Fori(RES_RING, BLOCKS - 2) as i:
                sp_block(i, has_out=True)
            sp_block(BLOCKS - 2, has_ctx=False, has_out=True)
            sp_block(BLOCKS - 1, has_ctx=False, has_next=False, has_out=True)
            sp.wait_ge(w_taken, 2 * UNITS - 4)
            load_mask(1, BLOCKS - 1)
            with sp.Fori(BLOCKS - RES_RING, BLOCKS) as i:
                store_out(i)
            sp.wait_ge(out_stored, 16 * BLOCKS)

        @block.tensor
        def _(pe):
            def passes(dst, pairs, last_sem):
                for j, (w, m) in enumerate(pairs):
                    mm = nc.tensor.matmul(dst, w, m, start=(j == 0), stop=(j == len(pairs) - 1))
                if last_sem is not None:
                    mm.then_inc(last_sem, 1)

            def project(l, what, m, filled):
                cols = slice((what * KT + m) * P, (what * KT + m + 1) * P)
                passes(proj[m][:, :],
                       [(w[:, k, cols], c[:, k, :]) for w, c in
                        ((w_in_lo[l], ctx_hi), (w_in_hi[l], ctx_lo), (w_in_hi[l], ctx_hi)) for k in range(KT)],
                       filled)

            def project_values(l, half):
                for j in range(2):
                    tok = slice((2 * half + j) * P, (2 * half + j + 1) * P)
                    passes(proj[half][:, j * CH:(j + 1) * CH],
                           [(c[:, k, tok], w[:, k, 2 * CH:3 * CH]) for w, c in
                            ((w_in_lo[l], ctx_hi), (w_in_hi[l], ctx_lo), (w_in_hi[l], ctx_hi)) for k in range(KT)],
                           v_filled if j == 1 else None)

            def project_out(l, m):
                passes(proj[m][:, :],
                       [(w[:, k, m * P:(m + 1) * P], o[:, k, :]) for w, o in
                        ((w_out_lo[l], o_hi), (w_out_hi[l], o_lo), (w_out_hi[l], o_hi)) for k in range(KT)],
                       w_filled)

            def fill(u, l, p, m, w_before):
                if p == 0:
                    if w_before:
                        pe.wait_ge(w_taken, 2 * u - 3 + m)
                    else:
                        pe.wait_ge(v_stored, 2 * u + 1 + m)
                    project(1 - l, 0, m, q_filled)
                elif p == 1:
                    pe.wait_ge(q_stored, 2 * u + 3 + m)
                    project(1 - l, 1, m, k_filled)
                elif p == 2:
                    pe.wait_ge(k_stored, 2 * u + 3 + m)
                    project_values(1 - l, m)

            def fill_out(u, l, m, v_before):
                if v_before:
                    pe.wait_ge(v_stored, 2 * u + 5 + m)
                else:
                    pe.wait_ge(w_taken, 2 * u - 1 + m)
                pe.wait_ge(o_lo_stored, 2 * u + 2)
                project_out(l, m)

            def transposes(s, j):
                pe.wait_ge(divided, s + 1)
                reached(pe, softT_stored, s - 1)
                flat = soft[j % SOFT][:, :, :].rearrange("p h k -> p (h k)")
                for hp in range(HEADS // 2):
                    t = nc.tensor.transpose(probsT[j % 2][:, hp * P:(hp + 1) * P], flat[:, hp * P:(hp + 1) * P], ident[:])
                t.then_inc(probsT_filled, 1)

            def score(s, u, l, p):
                if p == 0:
                    pe.wait_ge(q_stored, 2 * u + 2)
                    pe.wait_ge(k_stored, 2 * u + 2)
                reached(pe, masked, s - 1)
                for c in range(2):
                    tok = slice((2 * p + c) * CHUNK, (2 * p + c + 1) * CHUNK)
                    for g in range(KT):
                        w = HEADS_PER_TILE * CHUNK
                        mm = nc.tensor.matmul(scores[p % 2][c * CHUNK:(c + 1) * CHUNK, g * w:(g + 1) * w],
                                              q_sb[l][:, g, tok],
                                              k_sb[l][:, g, 2 * p + c].rearrange("p h k -> p (h k)"),
                                              start=True, stop=True)
                mm.then_inc(scores_filled, 1)

            def attend(s, u, l, p, j):
                if p == 0:
                    pe.wait_ge(v_stored, 2 * u + 2)
                    reached(pe, o_lo_stored, 2 * u)
                pe.wait_ge(softT_stored, s + 1)
                pe.sem_inc(pe_waited)
                for c in range(2):
                    for h in range(HEADS):
                        rows = slice(CHUNK * (h % 2), CHUNK * (h % 2) + CHUNK)
                        q4 = h % HEADS_PER_TILE
                        mm = nc.tensor.matmul(
                            att[h // HEADS_PER_TILE][q4 * HEAD_DIM:(q4 + 1) * HEAD_DIM,
                                                     p * P + c * CHUNK:p * P + (c + 1) * CHUNK],
                            v_sb[l][rows, p, c, (h // 2) * HEAD_DIM:(h // 2 + 1) * HEAD_DIM],
                            softT[j % 2][rows, h // 2, c * CHUNK:(c + 1) * CHUNK],
                            start=True, stop=True)
                mm.then_inc(att_filled, 1)

            def pe_block(i, first=False, last=False):
                for l in range(LAYERS):
                    for p in range(PAIRS):
                        j = 4 * l + p
                        s, u = 8 * i + j, 2 * i + l
                        lagged = not (first and j < 2)
                        lu, ll, lp = (u, l, p - 2) if p >= 2 else (u - 1, 1 - l, p + 2)
                        if lagged:
                            transposes(s - 2, j + 6)
                        for m in range(2):
                            if m == 1:
                                score(s, u, l, p)
                            if p == 3:
                                if not (first and l == 0):
                                    fill_out(u - 1, 1 - l, m, v_before=not (last and l == 1))
                            elif not (last and l == 1):
                                if l == 1 and p == 0 and m == 0:
                                    pe.wait_ge(ctx_lo_ready, i + 2)
                                fill(u, l, p, m, w_before=not first)
                        if lagged:
                            attend(s - 2, lu, ll, lp, j + 6)

            pe.wait_ge(w_lo_ready, 4)
            pe.wait_ge(ctx_lo_ready, 1)
            project(0, 0, 0, q_filled)
            project(0, 0, 1, q_filled)
            for m in range(2):
                fill(-1, 1, 1, m, False)
            for m in range(2):
                fill(-1, 1, 2, m, False)
            pe.wait_ge(ident_ready, 2)
            pe_block(0, first=True)
            with pe.Fori(1, BLOCKS - 1) as i:
                pe_block(i)
            pe_block(BLOCKS - 1, last=True)
            for p in range(2):
                transposes(STEPS - 2 + p, p + 6)
                attend(STEPS - 2 + p, UNITS - 1, 1, p + 2, p + 6)
            for m in range(2):
                fill_out(UNITS - 1, 1, m, v_before=False)

        @block.scalar
        def _(act):
            def split_ctx_hi(i, l0):
                act.wait_ge(ctx_loaded, 16 * (i + 1))
                if l0:
                    act.wait_ge(v_filled, 4 * i)
                nc.scalar.activation(ctx_hi[:], ctx_raw[:], ACT.Copy).then_inc(ctx_hi_ready, 1)

            def store_q(u, l, m):
                act.wait_ge(q_filled, 2 * u + m + 1)
                reached(act, scores_filled, 4 * u - 4)
                nc.scalar.activation(q_sb[l][:, m, :], proj[m][:, :], ACT.Identity, bias=bias_q[:, l, m:m + 1],
                                     scale=SCALE).then_inc(q_stored, 1)

            def store_k(u, l, m):
                act.wait_ge(k_filled, 2 * u + m + 1)
                reached(act, scores_filled, 4 * u - 4)
                for h in range(HEADS_PER_TILE):
                    rows = slice(h * HEAD_DIM, (h + 1) * HEAD_DIM)
                    c = nc.scalar.activation(k_sb[l][rows, m, :, h, :],
                                             proj[m][rows, :].rearrange("p (c k) -> p c k", k=CHUNK),
                                             ACT.Identity, bias=bias_in[rows, l, KT + m:KT + m + 1])
                c.then_inc(k_stored, 1)

            def store_v(u, l, half):
                act.wait_ge(v_filled, 2 * u + half + 1)
                reached(act, att_filled, 4 * u - 4)
                for c in range(2):
                    src = proj[half][c * CHUNK:(c + 1) * CHUNK, :]\
                        .rearrange("p (j h par d) -> p par j h d", j=2, par=2, d=HEAD_DIM)
                    for par in range(2):
                        dst = v_sb[l][par * CHUNK:(par + 1) * CHUNK, 2 * half:2 * half + 2, c, :]\
                            .rearrange("p j (h d) -> p j h d", d=HEAD_DIM)
                        v = nc.scalar.activation(dst, src[:, par], ACT.Copy)
                v.then_inc(v_stored, 1)

            def store_softT(s, j):
                act.wait_ge(probsT_filled, s + 1)
                reached(act, att_filled, s - 1)
                nc.scalar.activation(softT[j % 2][:, :, :].rearrange("p h q -> p (h q)"), probsT[j % 2][:, :],
                                     ACT.Copy).then_inc(softT_stored, 1)

            def exponentials(s, j):
                act.wait_ge(shifted, s + 1)
                nc.scalar.activation(soft[j % SOFT][:], soft[j % SOFT][:], ACT.Exp).then_inc(exp_done, 1)

            def store_o_hi(u, l):
                act.wait_ge(att_filled, 4 * u + 4)
                reached(act, w_filled, 2 * u)
                for g in range(KT):
                    nc.scalar.activation(o_hi[:, g, :], att[g][:, :], ACT.Identity,
                                         bias=bias_in[:, l, 2 * KT + g:2 * KT + g + 1]).then_inc(o_hi_stored, 1)

            def act_block(i, first=False, last=False):
                for l in range(LAYERS):
                    for p in range(PAIRS):
                        j = 4 * l + p
                        s, u = 8 * i + j, 2 * i + l
                        if p == 2 and not (first and l == 0):
                            store_o_hi(u - 1, 1 - l)
                        if not (first and j < 2):
                            store_softT(s - 2, j + 6)
                        if not (first and j < 1):
                            exponentials(s - 1, j + 7)
                        if not (last and l == 1) and p < 3:
                            for m in range(2):
                                (store_q, store_k, store_v)[p](u + 1, 1 - l, m)
                        if l == 0 and p == 3 and not last:
                            split_ctx_hi(i + 1, True)

            split_ctx_hi(0, False)
            act.wait_ge(w_loaded, 64)
            for l in range(LAYERS):
                nc.scalar.activation(w_in_hi[l][:], w_in_raw[l], ACT.Copy).then_inc(w_hi_ready, 1)
                nc.scalar.activation(w_out_hi[l][:], w_out_raw[l], ACT.Copy).then_inc(w_hi_ready, 1)
            act.wait_ge(bias_loaded, 64)
            act.wait_ge(bias_q_ready, 1)
            for m in range(2):
                store_q(0, 0, m)
            act.wait_ge(keys_zeroed, 2)
            for m in range(2):
                store_k(0, 0, m)
            for m in range(2):
                store_v(0, 0, m)
            act_block(0, first=True)
            with act.Fori(1, BLOCKS - 1) as i:
                act_block(i)
            act_block(BLOCKS - 1, last=True)
            store_softT(STEPS - 2, 6)
            exponentials(STEPS - 1, 7)
            store_softT(STEPS - 1, 7)
            store_o_hi(UNITS - 1, 1)

        @block.vector
        def _(dve):
            def split_ctx_lo(i):
                dve.wait_ge(ctx_hi_ready, i + 1)
                nc.vector.tensor_tensor(ctx_lo[:], ctx_raw[:], ctx_hi[:].bitcast(f32), ALU.subtract)\
                  .then_inc(ctx_lo_ready, 1)

            def store_o_lo(u, l):
                for g in range(KT):
                    dve.wait_ge(o_hi_stored, 2 * u + g + 1)
                    nc.vector.scalar_tensor_tensor(out=o_lo[:, g, :], in0=att[g][:, :],
                                                   scalar=bias_in[:, l, 2 * KT + g:2 * KT + g + 1],
                                                   in1=o_hi[:, g, :].bitcast(f32), op0=ALU.add,
                                                   op1=ALU.subtract).then_inc(o_lo_stored, 1)

            def sums(s, j):
                r = j % SOFT
                dve.wait_ge(exp_done, s + 1)
                nc.vector.reduce_sum(total[:, r, :], soft[r][:], AX.X).then_inc(totalled, 1)

            def invert(s, j):
                r = j % SOFT
                dve.wait_ge(totalled, s + 1)
                reached(dve, divided, s - 3)
                nc.vector.reciprocal(inv_total[:, r, :], total[:, r, :]).then_inc(inverted, 1)

            def shift(s, j, p):
                r = j % SOFT
                dve.wait_ge(scores_filled, s + 1)
                reached(dve, probsT_filled, s - 3)
                nc.vector.tensor_tensor(soft[r][:], scores[p % 2][:, :].rearrange("p (h k) -> p h k", k=CHUNK),
                                        key_neg[:, p, :].unsqueeze(1).to_broadcast([P, HEADS, CHUNK]),
                                        ALU.add).then_inc(masked, 1)
                dve.wait_ge(masked, s + 1)
                nc.vector.reduce_max(top[:, r, :], soft[r][:], AX.X).then_inc(topped, 1)
                dve.wait_ge(topped, s + 1)
                nc.vector.tensor_tensor(soft[r][:], soft[r][:],
                                        top[:, r, :].unsqueeze(2).to_broadcast([P, HEADS, CHUNK]),
                                        ALU.subtract).then_inc(shifted, 1)

            def take_layer0(i, b, m, recycled):
                dve.wait_ge(w_filled, 4 * i + m + 1)
                if m == 0:
                    dve.wait_ge(mask_loaded[0], 16 * (i + 1))
                    dve.wait_ge(x_loaded, 16 * (i + 1))
                nc.vector.scalar_tensor_tensor(out=masked_out[:, m, :], in0=proj[m][:, :], scalar=bias_out[:, 0, m:m + 1],
                                               in1=mask0[:], op0=ALU.add, op1=ALU.mult).then_inc(w_taken, 1)
                dve.wait_ge(w_taken, 4 * i + m + 1)
                if recycled and m == 0:
                    dve.wait_ge(out_stored, 16 * (i - RES_RING + 1))
                nc.vector.tensor_tensor(res[:, i % RES_RING, m, :], masked_out[:, m, :], x_raw[:, m, :], ALU.add)\
                  .then_inc(res_added, 1)
                dve.wait_ge(res_added, 2 * i + m + 1)
                nc.vector.bn_stats(stats[0][:, m, b, :], res[:, i % RES_RING, m, :]).then_inc(stats_done, 1)

            def take_layer1(i, m):
                dve.wait_ge(w_filled, 4 * i + m + 3)
                if m == 0:
                    dve.wait_ge(mask_loaded[1], 16 * (i + 1))
                nc.vector.scalar_tensor_tensor(out=att1[:, i % ATT_RING, m, :], in0=proj[m][:, :],
                                               scalar=bias_out[:, 1, m:m + 1], in1=mask1[:],
                                               op0=ALU.add, op1=ALU.mult).then_inc(w_taken, 1)

            def normalise(l, i, n, done):
                dve.wait_ge(rstd_ready, n)
                for m in range(KT):
                    r = nc.vector.tensor_scalar(res[:, i % RES_RING, m, :], res[:, i % RES_RING, m, :],
                                                mean_var[l][:, m, 0:1], rstd[:, l, m:m + 1],
                                                ALU.subtract, ALU.mult)
                r.then_inc(done, 1)

            def stats_layer1(i, b):
                dve.wait_ge(res1_added, i + 1)
                for m in range(KT):
                    nc.vector.bn_stats(stats[1][:, m, b, :], res[:, i % RES_RING, m, :]).then_inc(stats_done, 1)

            def aggregate(n, layers, stats_so_far):
                dve.wait_ge(stats_done, stats_so_far)
                dve.sem_inc(dve_waited)
                for l in layers:
                    for m in range(KT):
                        a = nc.vector.bn_aggr(mean_var[l][:, m, :], stats[l][:, m, :, :].rearrange("p b s -> p (b s)"))
                a.then_inc(aggregated, 1)
                dve.wait_ge(aggregated, n + 1)
                for l in layers:
                    v = nc.vector.tensor_scalar(var_eps[:, l, :], mean_var[l][:, :, 1], EPS, None, ALU.add)
                v.then_inc(var_ready, 1)

            def dve_block(i, n, b, first=False, last=False, norm0=False, norm1=False):
                dve.wait_ge(keymask_loaded, 32 * (i + 1))
                nc.vector.tensor_scalar(key_neg[:], key_mask[:], 0.0, NEG, ALU.is_le, ALU.mult)\
                  .then_inc(key_neg_ready, 1)
                for l in range(LAYERS):
                    for p in range(PAIRS):
                        j = 4 * l + p
                        s, u = 8 * i + j, 2 * i + l
                        if p == 2 and not (first and l == 0):
                            store_o_lo(u - 1, 1 - l)
                        if not (first and j == 0):
                            sums(s - 1, j + 7)
                            invert(s - 1, j + 7)
                        if p == 3:
                            if l == 1:
                                take_layer0(i, b, 0, recycled=norm1)
                            elif not first:
                                take_layer1(i - 1, 0)
                        if j == 0:
                            dve.wait_ge(key_neg_ready, i + 1)
                        shift(s, j, p)
                        if l == 0 and p == 3 and not last:
                            split_ctx_lo(i + 1)
                        if p == 3:
                            if l == 1:
                                take_layer0(i, b, 1, recycled=norm1)
                            elif not first:
                                take_layer1(i - 1, 1)
                        if j == 1 and norm1:
                            normalise(1, i - RES_RING, n, norm1_done)
                        if j == 4 and norm0:
                            normalise(0, i - ATT_RING, n, norm0_done)
                if norm0:
                    stats_layer1(i - ATT_RING, b)

            split_ctx_lo(0)
            for n, (lo, hi, raw) in enumerate([z for l in range(LAYERS) for z in
                                               ((w_in_lo[l], w_in_hi[l], w_in_raw[l]),
                                                (w_out_lo[l], w_out_hi[l], w_out_raw[l]))]):
                dve.wait_ge(w_hi_ready, n + 1)
                nc.vector.tensor_tensor(lo[:], raw, hi[:].bitcast(f32), ALU.subtract).then_inc(w_lo_ready, 1)
            dve.wait_ge(bias_loaded, 64)
            nc.vector.tensor_scalar(bias_q[:], bias_in[:, :, 0:KT], SCALE, None, ALU.mult).then_inc(bias_q_ready, 1)

            NB = BLOCKS_PER_BATCH
            dve_block(0, 0, 0, first=True)
            with dve.Fori(1, NB) as b:
                dve_block(b, 0, b)
            aggregate(0, [0], 2 * NB)
            with dve.Fori(0, NB) as b:
                dve_block(b + NB, 1, b, norm0=True)
            aggregate(1, [0, 1], 6 * NB)
            with dve.Fori(2, BATCH - 1) as n:
                with dve.Fori(0, NB) as b:
                    dve_block(dve.snap(n * NB + b), n, b, norm0=True, norm1=True)
                aggregate(n, [0, 1], (4 * n + 2) * NB)
            n = BATCH - 1
            with dve.Fori(0, NB - 1) as b:
                dve_block(b + n * NB, n, b, norm0=True, norm1=True)
            dve_block(BLOCKS - 1, n, NB - 1, last=True, norm0=True, norm1=True)
            aggregate(n, [0, 1], (4 * n + 2) * NB)
            sums(STEPS - 1, 7)
            invert(STEPS - 1, 7)
            store_o_lo(UNITS - 1, 1)
            for m in range(2):
                take_layer1(BLOCKS - 1, m)
            for b in range(NB):
                normalise(0, BLOCKS - NB + b, BATCH, norm0_done)
            for b in range(NB):
                normalise(1, BLOCKS - 2 * NB + b, BATCH, norm1_done)
            for b in range(NB):
                stats_layer1(BLOCKS - NB + b, b)
            aggregate(BATCH, [1], 4 * BLOCKS)
            for b in range(NB):
                normalise(1, BLOCKS - NB + b, BATCH + 1, norm1_done)

        @block.gpsimd
        def _(pool):
            def divide(s, j):
                r = j % SOFT
                pool.wait_ge(inverted, s + 1)
                nc.gpsimd.tensor_tensor(soft[r][:], soft[r][:],
                                        inv_total[:, r, :].unsqueeze(2).to_broadcast([P, HEADS, CHUNK]),
                                        ALU.mult).then_inc(divided, 1)

            def add_residual(i):
                pool.wait_ge(norm0_done, i + 1)
                pool.wait_ge(w_taken, 4 * i + 4)
                nc.gpsimd.tensor_tensor(res[:, i % RES_RING], res[:, i % RES_RING], att1[:, i % ATT_RING], ALU.add)\
                  .then_inc(res1_added, 1)

            def inverse_std(n, layers):
                pool.wait_ge(var_ready, n + 1)
                lo, hi = layers[0], layers[-1] + 1
                nc.gpsimd.tensor_tensor(rstd[:, lo:hi, :], var_eps[:, lo:hi, :], minus_half[:, lo:hi, :], ALU.pow)\
                  .then_inc(rstd_ready, 1)

            def pool_block(i, norm0=False):
                for j in range(2 * PAIRS):
                    divide(8 * i + j, j)
                    if norm0 and j == 4:
                        add_residual(i - ATT_RING)

            for l in range(LAYERS):
                nc.gpsimd.memset(k_sb[l][:], 0.0).then_inc(keys_zeroed, 1)
            nc.gpsimd.memset(minus_half[:], -0.5).then_inc(consts_ready, 1)
            nc.gpsimd.memset(ident[:], 0.0).then_inc(ident_ready, 1)
            pool.wait_ge(ident_ready, 1)
            nc.gpsimd.affine_select(out=ident[:], in_=ident[:], compare_op=ALU.not_equal, fill=1.0,
                                    base=0, pattern=[[-1, P]], channel_multiplier=1).then_inc(ident_ready, 1)
            pool.wait_ge(consts_ready, 1)
            NB = BLOCKS_PER_BATCH
            with pool.Fori(0, NB) as i:
                pool_block(i)
            inverse_std(0, [0])
            with pool.Fori(1, BATCH) as n:
                with pool.Fori(0, NB) as b:
                    pool_block(pool.snap(n * NB + b), norm0=True)
                inverse_std(n, [0, 1])
            with pool.Fori(BLOCKS - NB, BLOCKS) as i:
                add_residual(i)
            inverse_std(BATCH, [1])


def kernel(**inputs):
    import numpy as np
    import concourse.bacc as bacc
    from concourse.bass_utils import run_bass_kernel_spmd

    nc = bacc.Bacc("TRN2", target_bir_lowering=False, num_devices=1)
    arrays = {}

    def dram_in(name, a):
        arrays[name] = np.ascontiguousarray(a)
        return nc.dram_tensor(name, a.shape, mybir.dt.from_np(a.dtype), kind="ExternalInput").ap()

    x = dram_in("x_dram", np.asarray(inputs["x"]))
    ctx_in = dram_in("ctx_dram", np.asarray(inputs["ctx_4096"]))
    mask = dram_in("mask_dram", np.asarray(inputs["mask_Bx1x4096_ff1"]))
    w_in_t, b_in, w_out_t, b_out = [], [], [], []
    for l in range(LAYERS):
        w_in_t.append(dram_in(f"w_in_t{l}_dram", np.asarray(inputs[f"L{l}_xattn_W_in"]).T))
        b_in.append(dram_in(f"b_in{l}_dram", np.asarray(inputs[f"L{l}_xattn_b_in"]).reshape(-1, P).T))
        w_out_t.append(dram_in(f"w_out_t{l}_dram", np.asarray(inputs[f"L{l}_xattn_W_out"]).T))
        b_out.append(dram_in(f"b_out{l}_dram", np.asarray(inputs[f"L{l}_xattn_b_out"]).reshape(-1, P).T))
    out = nc.dram_tensor("out_dram", (BATCH, CH, TIME), mybir.dt.float32, kind="ExternalOutput").ap()
    build_attention(nc, x, ctx_in, mask, w_in_t, b_in, w_out_t, b_out, out)
    r = run_bass_kernel_spmd(nc, [arrays], core_ids=[0])
    return r.results[0]["out_dram"]
```

```python
import concourse.bass as bass
from concourse import mybir
from contextlib import ExitStack

BATCH, CH, TIME = 16, 256, 2048
HEADS, CHUNK = 8, 64
HEAD_DIM = CH // HEADS
LAYERS = 2
P = 128
KT = CH // P
BLK = 512
PAIRS = BLK // (2 * CHUNK)
CHUNKS = BLK // CHUNK
BLOCKS_PER_BATCH = TIME // BLK
BLOCKS = BATCH * BLOCKS_PER_BATCH
UNITS = BLOCKS * LAYERS
STEPS = UNITS * PAIRS
HEADS_PER_TILE = P // HEAD_DIM
SCALE = float(HEAD_DIM) ** -0.5
NEG = -1.0e9
EPS = 1.0e-5
SOFT = 4
RES_RING = 8
ATT_RING = 4


def build_attention(nc, x, ctx_in, mask, w_in_t, b_in, w_out_t, b_out, out):
    f32, f32r = mybir.dt.float32, mybir.dt.float32r
    ALU, ACT, AX = mybir.AluOpType, mybir.ActivationFunctionType, mybir.AxisListType

    ctx_blocks = ctx_in.rearrange("n (k p) (b t) -> n b p k t", p=P, t=BLK)
    x_blocks = x.rearrange("n (k p) (b t) -> n b p k t", p=P, t=BLK)
    out_blocks = out.rearrange("n (k p) (b t) -> n b p k t", p=P, t=BLK)
    mask_rows = mask.rearrange("n o (b t) -> n b (o t)", t=BLK)
    mask_keys = mask.rearrange("n o (b p c k) -> n b c (o p) k", p=PAIRS, c=2, k=CHUNK)

    with ExitStack() as es:
        def sb(name, shape, dt=f32):
            return es.enter_context(nc.sbuf_tensor(name, shape, dt))

        def pb(name):
            return es.enter_context(nc.psum_tensor(name, [P, 512], f32))

        def sem(name):
            return es.enter_context(nc.semaphore(name))

        w_in_hi = [sb(f"w_in_hi{l}", [P, KT, 3 * CH], f32r) for l in range(LAYERS)]
        w_in_lo = [sb(f"w_in_lo{l}", [P, KT, 3 * CH], f32r) for l in range(LAYERS)]
        w_out_hi = [sb(f"w_out_hi{l}", [P, KT, CH], f32r) for l in range(LAYERS)]
        w_out_lo = [sb(f"w_out_lo{l}", [P, KT, CH], f32r) for l in range(LAYERS)]
        bias_in = sb("bias_in", [P, LAYERS, 3 * KT])
        bias_q = sb("bias_q", [P, LAYERS, KT])
        bias_out = sb("bias_out", [P, LAYERS, KT])
        ident = sb("ident", [P, P])
        ctx_raw = sb("ctx_raw", [P, KT, BLK])
        ctx_hi = sb("ctx_hi", [P, KT, BLK], f32r)
        ctx_lo = sb("ctx_lo", [P, KT, BLK], f32r)
        x_raw = sb("x_raw", [P, KT, BLK])
        q_sb = [sb(f"q{l}", [P, KT, BLK]) for l in range(LAYERS)]
        k_sb = [sb(f"k{l}", [P, KT, CHUNKS, HEADS_PER_TILE, CHUNK]) for l in range(LAYERS)]
        v_sb = [sb(f"v{l}", [P, PAIRS, 2, HEADS // 2, 2, HEAD_DIM]) for l in range(LAYERS)]
        soft = [sb(f"soft{j}", [P, HEADS, CHUNK]) for j in range(SOFT)]
        softT = [sb(f"softT{j}", [P, HEADS // 2, P]) for j in range(2)]
        top = sb("top", [P, SOFT, HEADS])
        total = sb("total", [P, SOFT, HEADS])
        inv_total = sb("inv_total", [P, SOFT, HEADS])
        o_hi = sb("o_hi", [P, KT, BLK], f32r)
        o_lo = sb("o_lo", [P, KT, BLK], f32r)
        mask0 = sb("mask0", [P, BLK])
        mask1 = sb("mask1", [P, BLK])
        mask_bc = [mask0, mask1]
        key_mask = sb("key_mask", [P, PAIRS, CHUNK])
        key_neg = sb("key_neg", [P, PAIRS, CHUNK])
        masked_out = sb("masked_out", [P, KT, BLK])
        res = sb("res", [P, RES_RING, KT, BLK])
        att1 = sb("att1", [P, ATT_RING, KT, BLK])
        stats = [sb(f"stats{l}", [P, KT, BLOCKS_PER_BATCH, 6]) for l in range(LAYERS)]
        mean_var = [sb(f"mean_var{l}", [P, KT, 2]) for l in range(LAYERS)]
        var_eps = sb("var_eps", [P, LAYERS, KT])
        rstd = sb("rstd", [P, LAYERS, KT])
        neg_mean = sb("neg_mean", [P, KT])
        minus_half = sb("minus_half", [P, LAYERS, KT])

        scores = [pb("scores0"), pb("scores1")]
        proj = [pb("proj0"), pb("proj1")]
        probsT = [pb("probsT0"), pb("probsT1")]
        att = [pb("att0"), pb("att1_ps")]

        stage = res[:, :, :, :].rearrange("p a k t -> p (a k t)")
        PER_LAYER = KT * 3 * CH + KT * CH
        w_in_raw = [stage[:, l * PER_LAYER:l * PER_LAYER + KT * 3 * CH].rearrange("p (k n) -> p k n", k=KT)
                    for l in range(LAYERS)]
        w_out_raw = [stage[:, l * PER_LAYER + KT * 3 * CH:(l + 1) * PER_LAYER].rearrange("p (k n) -> p k n", k=KT)
                     for l in range(LAYERS)]

        w_loaded, bias_loaded = [sem(f"w_loaded{k}") for k in range(4)], sem("bias_loaded")
        ctx_loaded, x_loaded, keymask_loaded = sem("ctx_loaded"), sem("x_loaded"), sem("keymask_loaded")
        mask_loaded = [sem("mask0_loaded"), sem("mask1_loaded")]
        out_stored = sem("out_stored")
        keys0_zeroed, keys1_zeroed, values_zeroed = sem("keys0_zeroed"), sem("keys1_zeroed"), sem("values_zeroed")
        ident_ready, consts_ready = sem("ident_ready"), sem("consts_ready")
        w_hi_ready, w_lo_ready, bias_q_ready = sem("w_hi_ready"), sem("w_lo_ready"), sem("bias_q_ready")
        q_filled, k_filled, v_filled, w_filled = sem("q_filled"), sem("k_filled"), sem("v_filled"), sem("w_filled")
        scores_filled, probsT_filled, att_filled = sem("scores_filled"), sem("probsT_filled"), sem("att_filled")
        q_stored, k_stored, v_stored, o_hi_stored = sem("q_stored"), sem("k_stored"), sem("v_stored"), sem("o_hi_stored")
        ctx_hi_ready, exp_done, softT_stored = sem("ctx_hi_ready"), sem("exp_done"), sem("softT_stored")
        masked, topped, shifted = sem("masked"), sem("topped"), sem("shifted")
        totalled, inverted = sem("totalled"), sem("inverted")
        o_lo_stored, w_taken, key_neg_ready = sem("o_lo_stored"), sem("w_taken"), sem("key_neg_ready")
        stats_done, aggregated, var_ready = sem("stats_done"), sem("aggregated"), sem("var_ready")
        norm0_done, norm1_done, last_res1_added = sem("norm0_done"), sem("norm1_done"), sem("last_res1_added")
        neg_mean_ready, centred, act_norm1_done = sem("neg_mean_ready"), sem("centred"), sem("act_norm1_done")
        divided, x_added, res1_added = sem("divided"), sem("x_added"), sem("res1_added")
        ctx_lo_ready, rstd_ready = sem("ctx_lo_ready"), sem("rstd_ready")

        dve_waited = sem("dve_waited")

        block = es.enter_context(nc.Block())

        def exists(index, count):
            return not isinstance(index, int) or 0 <= index < count

        def reached(eng, semaphore, count):
            if not (isinstance(count, int) and count <= 0):
                eng.wait_ge(semaphore, count)

        @block.sync
        def _(sp):
            def at(blocks, i):
                return blocks[i // BLOCKS_PER_BATCH, i % BLOCKS_PER_BATCH]

            def load_ctx(i):
                sp.dma_start(ctx_raw[:], at(ctx_blocks, i)).then_inc(ctx_loaded, 16)

            def load_key_mask(i):
                for c in range(2):
                    sp.dma_start(key_mask[c * CHUNK:(c + 1) * CHUNK], at(mask_keys, i)[c].partition_broadcast(CHUNK))\
                      .then_inc(keymask_loaded, 16)

            def load_mask(l, i):
                sp.dma_start(mask_bc[l][:], at(mask_rows, i).partition_broadcast(P)).then_inc(mask_loaded[l], 16)

            def store_out(i, done=norm1_done, before=0):
                sp.wait_ge(done, i + 1 - before)
                sp.dma_start(at(out_blocks, i), res[:, i % RES_RING]).then_inc(out_stored, 16)

            def sp_block(r, norm1=False):
                reached(sp, x_added, r)
                sp.dma_start(x_raw[:], at(x_blocks, r)).then_inc(x_loaded, 16)
                if exists(r + 2, BLOCKS):
                    sp.wait_ge(key_neg_ready, r + 2)
                    load_key_mask(r + 2)
                sp.wait_ge(w_taken, 4 * r + 2)
                load_mask(1, r)
                if exists(r + 1, BLOCKS):
                    load_mask(0, r + 1)
                if norm1:
                    store_out(r - RES_RING)
                if exists(r + 3, BLOCKS):
                    sp.wait_ge(ctx_lo_ready, r + 3)
                    load_ctx(r + 3)

            load_ctx(0)
            sp.dma_start(w_in_raw[0], w_in_t[0].rearrange("(k p) n -> p k n", p=P)).then_inc(w_loaded[0], 16)
            for l in range(LAYERS):
                sp.dma_start(bias_in[:, l], b_in[l]).then_inc(bias_loaded, 16)
                sp.dma_start(bias_out[:, l], b_out[l]).then_inc(bias_loaded, 16)
            sp.dma_start(w_in_raw[1], w_in_t[1].rearrange("(k p) n -> p k n", p=P)).then_inc(w_loaded[1], 16)
            load_key_mask(0)
            for l in range(LAYERS):
                sp.dma_start(w_out_raw[l], w_out_t[l].rearrange("(k p) n -> p k n", p=P)).then_inc(w_loaded[2 + l], 16)
            load_mask(0, 0)
            sp.wait_ge(key_neg_ready, 1)
            load_key_mask(1)
            for i in range(2):
                sp.wait_ge(ctx_lo_ready, i + 1)
                load_ctx(i + 1)
            sp_block(0)
            with sp.Fori(1, RES_RING) as r:
                sp_block(r)
            with sp.Fori(RES_RING, BLOCKS - 3) as r:
                sp_block(r, norm1=True)
            for r in range(BLOCKS - 3, BLOCKS):
                sp_block(r, norm1=True)
            for i in range(BLOCKS - 2 * BLOCKS_PER_BATCH, BLOCKS - BLOCKS_PER_BATCH):
                store_out(i, act_norm1_done, BLOCKS - 2 * BLOCKS_PER_BATCH)
            for i in range(BLOCKS - BLOCKS_PER_BATCH, BLOCKS):
                store_out(i, norm1_done, BLOCKS_PER_BATCH)
            sp.wait_ge(out_stored, 16 * BLOCKS)

        @block.tensor
        def _(pe):
            def passes(dst, products, filled=None):
                for j, (w, m) in enumerate(products):
                    mm = nc.tensor.matmul(dst, w, m, start=(j == 0), stop=(j == len(products) - 1))
                if filled is not None:
                    mm.then_inc(filled, 1)

            def project(l, what, m, bank, filled):
                cols = slice((what * KT + m) * P, (what * KT + m + 1) * P)
                passes(proj[bank][:, :],
                       [(w[:, k, cols], c[:, k, :]) for w, c in
                        ((w_in_lo[l], ctx_hi), (w_in_hi[l], ctx_lo), (w_in_hi[l], ctx_hi)) for k in range(KT)],
                       filled)

            def project_values(l, half):
                for j in range(2):
                    tok = slice((2 * half + j) * P, (2 * half + j + 1) * P)
                    passes(proj[half][:, j * CH:(j + 1) * CH],
                           [(c[:, k, tok], w[:, k, 2 * CH:3 * CH]) for w, c in
                            ((w_in_lo[l], ctx_hi), (w_in_hi[l], ctx_lo), (w_in_hi[l], ctx_hi)) for k in range(KT)],
                           v_filled if j == 1 else None)

            def fill_in(u, l, p, bank):
                if p == 1:
                    if exists(u - 3, UNITS):
                        pe.wait_ge(w_taken, 2 * u - 5 + bank)
                    else:
                        reached(pe, v_stored, 2 * u - 1 + bank)
                else:
                    pe.wait_ge((k_stored, q_stored)[bank], 2 * u + p - 1)
                if p < 3:
                    project(l, 1 - bank, p - 1, bank, (k_filled, q_filled)[bank])
                else:
                    project_values(l, bank)

            def fill_out(u, l, m):
                if exists(u + 2, UNITS):
                    pe.wait_ge(v_stored, 2 * u + 5 + m)
                elif exists(u + 1, UNITS):
                    pe.wait_ge(v_stored, 2 * u + 3 + m)
                else:
                    pe.wait_ge(w_taken, 2 * u - 1 + m)
                pe.wait_ge(o_lo_stored, 2 * u + 2)
                passes(proj[m][:, :],
                       [(w[:, k, m * P:(m + 1) * P], o[:, k, :]) for w, o in
                        ((w_out_lo[l], o_hi), (w_out_hi[l], o_lo), (w_out_hi[l], o_hi)) for k in range(KT)],
                       w_filled)

            def transposes(s, j):
                pe.wait_ge(divided, s + 1)
                reached(pe, softT_stored, s - 1)
                flat = soft[j % SOFT][:, :, :].rearrange("p h k -> p (h k)")
                for hp in range(HEADS // 2):
                    t = nc.tensor.transpose(probsT[j % 2][:, hp * P:(hp + 1) * P], flat[:, hp * P:(hp + 1) * P], ident[:])
                t.then_inc(probsT_filled, 1)

            def score(s, u, l, p):
                if p == 0:
                    pe.wait_ge(q_stored, 2 * u + 2)
                    pe.wait_ge(k_stored, 2 * u + 2)
                reached(pe, masked, s - 1)
                w = HEADS_PER_TILE * CHUNK
                for c in range(2):
                    tok = slice((2 * p + c) * CHUNK, (2 * p + c + 1) * CHUNK)
                    for g in range(KT):
                        mm = nc.tensor.matmul(scores[p % 2][c * CHUNK:(c + 1) * CHUNK, g * w:(g + 1) * w],
                                              q_sb[l][:, g, tok],
                                              k_sb[l][:, g, 2 * p + c].rearrange("p h k -> p (h k)"),
                                              start=True, stop=True)
                mm.then_inc(scores_filled, 1)

            def attend(s, u, l, p, j):
                if p == 0:
                    pe.wait_ge(v_stored, 2 * u + 2)
                    reached(pe, o_lo_stored, 2 * u)
                pe.wait_ge(softT_stored, s + 1)
                for hp in range(HEADS // 2):
                    for c in range(2):
                        mm = nc.tensor.matmul(
                            att[hp // 2][(hp % 2) * CHUNK:(hp % 2 + 1) * CHUNK,
                                         p * P + c * CHUNK:p * P + (c + 1) * CHUNK],
                            v_sb[l][:, p, c, hp].rearrange("p par d -> p (par d)"),
                            softT[j % 2][:, hp, c * CHUNK:(c + 1) * CHUNK],
                            start=True, stop=True)
                mm.then_inc(att_filled, 1)

            def pe_block(i, steps=range(2 * PAIRS)):
                for j in steps:
                    l, p = j // PAIRS, j % PAIRS
                    s, u = 8 * i + j, 2 * i + l
                    if exists(s, STEPS):
                        score(s, u, l, p)
                    if exists(s - 3, STEPS):
                        transposes(s - 3, j + 5)
                    if j == 5 and exists(i + 1, BLOCKS):
                        pe.wait_ge(ctx_lo_ready, i + 2)
                    for bank in range(2):
                        if p == 0 and exists(u - 2, UNITS):
                            fill_out(u - 2, l, bank)
                        elif p > 0 and exists(u + 1, UNITS):
                            fill_in(u + 1, 1 - l, p, bank)
                    if exists(s - 3, STEPS):
                        if p == 3:
                            attend(s - 3, u, l, 0, j + 5)
                        else:
                            attend(s - 3, u - 1, 1 - l, p + 1, j + 5)

            pe.wait_ge(w_lo_ready, 1)
            pe.wait_ge(ctx_lo_ready, 1)
            for p in range(1, PAIRS):
                for bank in range(2):
                    fill_in(0, 0, p, bank)
            pe.wait_ge(w_lo_ready, 4)
            pe.wait_ge(ident_ready, 2)
            pe_block(0)
            with pe.Fori(1, BLOCKS - 1) as i:
                pe_block(i)
            pe_block(BLOCKS - 1)
            pe_block(BLOCKS, range(3))
            for m in range(KT):
                fill_out(UNITS - 1, 1, m)

        @block.scalar
        def _(act):
            def split_ctx_hi(i):
                act.wait_ge(ctx_loaded, 16 * (i + 1))
                reached(act, v_filled, 4 * i)
                nc.scalar.activation(ctx_hi[:], ctx_raw[:], ACT.Copy).then_inc(ctx_hi_ready, 1)

            def store_q(u, l, m):
                act.wait_ge(q_filled, 2 * u + m + 1)
                reached(act, scores_filled, 4 * u - 4)
                nc.scalar.activation(q_sb[l][:, m, :], proj[1][:, :], ACT.Identity, bias=bias_q[:, l, m:m + 1],
                                     scale=SCALE).then_inc(q_stored, 1)

            def store_k(u, l, m):
                act.wait_ge(k_filled, 2 * u + m + 1)
                reached(act, scores_filled, 4 * u - 4)
                for h in range(HEADS_PER_TILE):
                    rows = slice(h * HEAD_DIM, (h + 1) * HEAD_DIM)
                    c = nc.scalar.activation(k_sb[l][rows, m, :, h, :],
                                             proj[0][rows, :].rearrange("p (c k) -> p c k", k=CHUNK),
                                             ACT.Identity, bias=bias_in[rows, l, KT + m:KT + m + 1])
                c.then_inc(k_stored, 1)

            def store_v(u, l, half):
                act.wait_ge(v_filled, 2 * u + half + 1)
                reached(act, att_filled, 4 * u - 4)
                for c in range(2):
                    src = proj[half][c * CHUNK:(c + 1) * CHUNK, :]\
                        .rearrange("p (j h par d) -> p par j h d", j=2, par=2, d=HEAD_DIM)
                    for par in range(2):
                        dst = v_sb[l][par * CHUNK:(par + 1) * CHUNK, 2 * half:2 * half + 2, c, :, par, :]
                        v = nc.scalar.activation(dst, src[:, par], ACT.Copy)
                v.then_inc(v_stored, 1)

            def store_in(u, l, p):
                if p < 3:
                    store_k(u, l, p - 1)
                    store_q(u, l, p - 1)
                else:
                    for half in range(2):
                        store_v(u, l, half)

            def store_softT(s, j):
                act.wait_ge(probsT_filled, s + 1)
                reached(act, att_filled, s - 1)
                nc.scalar.activation(softT[j % 2][:, :, :].rearrange("p h q -> p (h q)"), probsT[j % 2][:, :],
                                     ACT.Copy).then_inc(softT_stored, 1)

            def exponentials(s, j):
                act.wait_ge(shifted, s + 1)
                nc.scalar.activation(soft[j % SOFT][:], soft[j % SOFT][:], ACT.Exp).then_inc(exp_done, 1)

            def store_o_hi(u, l):
                act.wait_ge(att_filled, 4 * u + 4)
                reached(act, w_filled, 2 * u)
                for g in range(KT):
                    nc.scalar.activation(o_hi[:, g, :], att[g][:, :], ACT.Identity,
                                         bias=bias_in[:, l, 2 * KT + g:2 * KT + g + 1]).then_inc(o_hi_stored, 1)

            def act_block(i, steps=range(2 * PAIRS)):
                for j in steps:
                    l, p = j // PAIRS, j % PAIRS
                    s, u = 8 * i + j, 2 * i + l
                    if p == 3 and exists(u - 1, UNITS):
                        store_o_hi(u - 1, 1 - l)
                    if exists(s - 3, STEPS):
                        store_softT(s - 3, j + 5)
                    if exists(s - 1, STEPS - 1):
                        exponentials(s - 1, j + 7)
                    if j == 4 and exists(i + 1, BLOCKS):
                        split_ctx_hi(i + 1)
                    if p > 0 and exists(u + 1, UNITS):
                        store_in(u + 1, 1 - l, p)

            split_ctx_hi(0)
            for l in range(LAYERS):
                act.wait_ge(w_loaded[l], 16)
                nc.scalar.activation(w_in_hi[l][:], w_in_raw[l], ACT.Copy).then_inc(w_hi_ready, 1)
            for l in range(LAYERS):
                act.wait_ge(w_loaded[2 + l], 16)
                nc.scalar.activation(w_out_hi[l][:], w_out_raw[l], ACT.Copy).then_inc(w_hi_ready, 1)
            act.wait_ge(bias_loaded, 64)
            act.wait_ge(bias_q_ready, 1)
            act.wait_ge(keys0_zeroed, 1)
            act.wait_ge(keys1_zeroed, 1)
            for m in range(KT):
                store_k(0, 0, m)
            act.wait_ge(values_zeroed, 2)
            for half in range(2):
                store_v(0, 0, half)
            act_block(0)
            with act.Fori(1, BLOCKS - 1) as i:
                act_block(i)
            act_block(BLOCKS - 1)
            exponentials(STEPS - 1, 2 * PAIRS - 1)
            act_block(BLOCKS, range(4))
            act.wait_ge(neg_mean_ready, 1)
            act.wait_ge(rstd_ready, BATCH)
            for b in range(BLOCKS_PER_BATCH):
                i = BLOCKS - 2 * BLOCKS_PER_BATCH + b
                for m in range(KT):
                    nc.scalar.activation(res[:, i % RES_RING, m, :], res[:, i % RES_RING, m, :], ACT.Identity,
                                         bias=neg_mean[:, m:m + 1]).then_inc(centred, 1)
                act.wait_ge(centred, KT * (b + 1))
                for m in range(KT):
                    a = nc.scalar.activation(res[:, i % RES_RING, m, :], res[:, i % RES_RING, m, :], ACT.Copy,
                                             scale=rstd[:, 1, m:m + 1])
                a.then_inc(act_norm1_done, 1)

        @block.vector
        def _(dve):
            def make_key_neg(i):
                dve.wait_ge(keymask_loaded, 32 * (i + 1))
                nc.vector.tensor_scalar(key_neg[:], key_mask[:], 0.0, NEG, ALU.is_le, ALU.mult)\
                  .then_inc(key_neg_ready, 1)

            def store_o_lo(u, l):
                for g in range(KT):
                    dve.wait_ge(o_hi_stored, 2 * u + g + 1)
                    nc.vector.scalar_tensor_tensor(out=o_lo[:, g, :], in0=att[g][:, :],
                                                   scalar=bias_in[:, l, 2 * KT + g:2 * KT + g + 1],
                                                   in1=o_hi[:, g, :].bitcast(f32), op0=ALU.add,
                                                   op1=ALU.subtract).then_inc(o_lo_stored, 1)

            def sums(s, j):
                dve.wait_ge(exp_done, s + 1)
                nc.vector.reduce_sum(total[:, j % SOFT, :], soft[j % SOFT][:], AX.X).then_inc(totalled, 1)

            def invert(s, j):
                dve.wait_ge(totalled, s + 1)
                reached(dve, divided, s - 3)
                nc.vector.reciprocal(inv_total[:, j % SOFT, :], total[:, j % SOFT, :]).then_inc(inverted, 1)

            def mask_scores(s, j, p):
                dve.wait_ge(scores_filled, s + 1)
                reached(dve, probsT_filled, s - 3)
                nc.vector.tensor_tensor(soft[j % SOFT][:], scores[p % 2][:, :].rearrange("p (h k) -> p h k", k=CHUNK),
                                        key_neg[:, p, :].unsqueeze(1).to_broadcast([P, HEADS, CHUNK]),
                                        ALU.add).then_inc(masked, 1)

            def maxima(s, j):
                dve.wait_ge(masked, s + 1)
                nc.vector.reduce_max(top[:, j % SOFT, :], soft[j % SOFT][:], AX.X).then_inc(topped, 1)

            def shift(s, j):
                dve.wait_ge(topped, s + 1)
                nc.vector.tensor_tensor(soft[j % SOFT][:], soft[j % SOFT][:],
                                        top[:, j % SOFT, :].unsqueeze(2).to_broadcast([P, HEADS, CHUNK]),
                                        ALU.subtract).then_inc(shifted, 1)

            def take_out(l, r):
                dve.wait_ge(mask_loaded[l], 16 * (r + 1))
                for m in range(KT):
                    dve.wait_ge(w_filled, 4 * r + 2 * l + m + 1)
                    dst = masked_out[:, m, :] if l == 0 else att1[:, r % ATT_RING, m, :]
                    nc.vector.scalar_tensor_tensor(out=dst, in0=proj[m][:, :], scalar=bias_out[:, l, m:m + 1],
                                                   in1=mask_bc[l][:], op0=ALU.add, op1=ALU.mult)\
                      .then_inc(w_taken, 1)

            def normalise(l, i, n, done):
                dve.wait_ge(rstd_ready, n)
                for m in range(KT):
                    r = nc.vector.tensor_scalar(res[:, i % RES_RING, m, :], res[:, i % RES_RING, m, :],
                                                mean_var[l][:, m, 0:1], rstd[:, l, m:m + 1],
                                                ALU.subtract, ALU.mult)
                r.then_inc(done, 1)

            def statistics(l, i, b):
                for m in range(KT):
                    nc.vector.bn_stats(stats[l][:, m, b, :], res[:, i % RES_RING, m, :]).then_inc(stats_done, 1)

            def aggregate(n, layers, stats_so_far):
                dve.wait_ge(stats_done, stats_so_far)
                dve.sem_inc(dve_waited)
                for l in layers:
                    for m in range(KT):
                        a = nc.vector.bn_aggr(mean_var[l][:, m, :], stats[l][:, m, :, :].rearrange("p b s -> p (b s)"))
                a.then_inc(aggregated, 1)
                dve.wait_ge(aggregated, n + 1)
                for l in layers:
                    v = nc.vector.tensor_scalar(var_eps[:, l, :], mean_var[l][:, :, 1], EPS, None, ALU.add)
                v.then_inc(var_ready, 1)

            def dve_block(i, n=None, b=None, steps=range(2 * PAIRS), norm0=False, norm1=False):
                r = i - 1
                for j in steps:
                    l, p = j // PAIRS, j % PAIRS
                    s, u = 8 * i + j, 2 * i + l
                    if exists(s - 2, STEPS):
                        sums(s - 2, j + 6)
                    if exists(s, STEPS):
                        mask_scores(s, j, p)
                    if exists(s - 2, STEPS):
                        invert(s - 2, j + 6)
                    if p == 3 and exists(u - 1, UNITS):
                        store_o_lo(u - 1, 1 - l)
                    if exists(s, STEPS):
                        maxima(s, j)
                    if j == 1 and norm0:
                        normalise(0, r - ATT_RING, n, norm0_done)
                    if j == 5 and b is not None:
                        dve.wait_ge(x_added, r + 1)
                        statistics(0, r, b)
                    if j == 6 and norm0:
                        dve.wait_ge(res1_added, r - ATT_RING + 1)
                        statistics(1, r - ATT_RING, b)
                    if exists(s, STEPS):
                        shift(s, j)
                    if j == 0 and b is not None:
                        take_out(0, r)
                        if norm1:
                            normalise(1, r - RES_RING, n, norm1_done)
                    if j == 4 and b is not None:
                        if norm0:
                            dve.wait_ge(res1_added, r - ATT_RING + 1)
                        take_out(1, r)
                    if j == 7 and exists(i + 1, BLOCKS):
                        make_key_neg(i + 1)
                        dve.wait_ge(key_neg_ready, i + 2)

            nc.vector.memset(k_sb[0][:], 0.0).then_inc(keys0_zeroed, 1)
            for k, (lo, hi, raw) in enumerate([(w_in_lo[l], w_in_hi[l], w_in_raw[l]) for l in range(LAYERS)] +
                                              [(w_out_lo[l], w_out_hi[l], w_out_raw[l]) for l in range(LAYERS)]):
                dve.wait_ge(w_hi_ready, k + 1)
                nc.vector.tensor_tensor(lo[:], raw, hi[:].bitcast(f32), ALU.subtract).then_inc(w_lo_ready, 1)
                if k == 0:
                    dve.wait_ge(bias_loaded, 64)
                    nc.vector.tensor_scalar(bias_q[:], bias_in[:, :, 0:KT], SCALE, None, ALU.mult)\
                      .then_inc(bias_q_ready, 1)
            make_key_neg(0)
            dve.wait_ge(key_neg_ready, 1)
            for m in range(KT):
                dve.wait_ge(q_filled, m + 1)
                nc.vector.tensor_scalar(q_sb[0][:, m, :], proj[1][:, :], bias_in[:, 0, m:m + 1], SCALE,
                                        ALU.add, ALU.mult).then_inc(q_stored, 1)

            NB = BLOCKS_PER_BATCH
            dve_block(0)
            with dve.Fori(0, NB) as b:
                dve_block(b + 1, 0, b)
            aggregate(0, [0], 2 * NB)
            with dve.Fori(0, NB) as b:
                dve_block(b + NB + 1, 1, b, norm0=True)
            aggregate(1, [0, 1], 6 * NB)
            with dve.Fori(2, BATCH - 1) as n:
                with dve.Fori(0, NB) as b:
                    dve_block(dve.snap(n * NB + b + 1), n, b, norm0=True, norm1=True)
                aggregate(n, [0, 1], (4 * n + 2) * NB)
            n = BATCH - 1
            with dve.Fori(0, NB - 2) as b:
                dve_block(b + n * NB + 1, n, b, norm0=True, norm1=True)
            dve_block(BLOCKS - 1, n, NB - 2, norm0=True, norm1=True)
            dve_block(BLOCKS, steps=range(2))
            normalise(0, BLOCKS - 1 - ATT_RING, n, norm0_done)
            take_out(0, BLOCKS - 1)
            normalise(1, BLOCKS - 1 - RES_RING, n, norm1_done)
            store_o_lo(UNITS - 1, 1)
            dve.wait_ge(x_added, BLOCKS)
            statistics(0, BLOCKS - 1, NB - 1)
            dve.wait_ge(res1_added, BLOCKS - ATT_RING)
            statistics(1, BLOCKS - 1 - ATT_RING, NB - 1)
            aggregate(n, [0, 1], (4 * n + 2) * NB)
            nc.vector.tensor_scalar(neg_mean[:], mean_var[1][:, :, 0], -1.0, None, ALU.mult)\
              .then_inc(neg_mean_ready, 1)
            for b in range(NB):
                normalise(0, BLOCKS - NB + b, BATCH, norm0_done)
            take_out(1, BLOCKS - 1)
            dve.wait_ge(norm0_done, BLOCKS)
            dve.wait_ge(w_taken, 2 * UNITS)
            nc.vector.tensor_tensor(res[:, (BLOCKS - 1) % RES_RING], res[:, (BLOCKS - 1) % RES_RING],
                                    att1[:, (BLOCKS - 1) % ATT_RING], ALU.add).then_inc(last_res1_added, 1)
            for b in range(NB - 1):
                dve.wait_ge(res1_added, BLOCKS - NB + b + 1)
                statistics(1, BLOCKS - NB + b, b)
            dve.wait_ge(last_res1_added, 1)
            statistics(1, BLOCKS - 1, NB - 1)
            dve.wait_ge(neg_mean_ready, 1)
            aggregate(BATCH, [1], 4 * BLOCKS)
            for b in range(NB):
                normalise(1, BLOCKS - NB + b, BATCH + 1, norm1_done)

        @block.gpsimd
        def _(pool):
            def split_ctx_lo(i):
                pool.wait_ge(ctx_hi_ready, i + 1)
                nc.gpsimd.tensor_tensor(ctx_lo[:], ctx_raw[:], ctx_hi[:].bitcast(f32), ALU.subtract)\
                  .then_inc(ctx_lo_ready, 1)

            def divide(s, j):
                pool.wait_ge(inverted, s + 1)
                nc.gpsimd.tensor_tensor(soft[j % SOFT][:], soft[j % SOFT][:],
                                        inv_total[:, j % SOFT, :].unsqueeze(2).to_broadcast([P, HEADS, CHUNK]),
                                        ALU.mult).then_inc(divided, 1)

            def add_x(r, recycled):
                pool.wait_ge(w_taken, 4 * r + 2)
                pool.wait_ge(x_loaded, 16 * (r + 1))
                if recycled:
                    pool.wait_ge(out_stored, 16 * (r - RES_RING + 1))
                nc.gpsimd.tensor_tensor(res[:, r % RES_RING], masked_out[:], x_raw[:], ALU.add).then_inc(x_added, 1)

            def add_residual(i):
                pool.wait_ge(norm0_done, i + 1)
                pool.wait_ge(w_taken, 4 * i + 4)
                nc.gpsimd.tensor_tensor(res[:, i % RES_RING], res[:, i % RES_RING], att1[:, i % ATT_RING], ALU.add)\
                  .then_inc(res1_added, 1)

            def inverse_std(n, lo, hi):
                pool.wait_ge(var_ready, n + 1)
                nc.gpsimd.tensor_tensor(rstd[:, lo:hi, :], var_eps[:, lo:hi, :], minus_half[:, lo:hi, :], ALU.pow)\
                  .then_inc(rstd_ready, 1)

            def pool_block(i, residuals=True, norm0=False, norm1=False):
                for j in range(2 * PAIRS):
                    s = 8 * i + j
                    if exists(s - 2, STEPS):
                        divide(s - 2, j + 6)
                    if j == 2 and norm0:
                        add_residual(i - 1 - ATT_RING)
                    if j == 3 and residuals:
                        add_x(i - 1, recycled=norm1)
                    if j == 4 and exists(i + 1, BLOCKS):
                        split_ctx_lo(i + 1)

            split_ctx_lo(0)
            nc.gpsimd.memset(k_sb[1][:], 0.0).then_inc(keys1_zeroed, 1)
            for l in range(LAYERS):
                nc.gpsimd.memset(v_sb[l][:], 0.0).then_inc(values_zeroed, 1)
            nc.gpsimd.memset(minus_half[:], -0.5).then_inc(consts_ready, 1)
            nc.gpsimd.memset(ident[:], 0.0).then_inc(ident_ready, 1)
            pool.wait_ge(ident_ready, 1)
            nc.gpsimd.affine_select(out=ident[:], in_=ident[:], compare_op=ALU.not_equal, fill=1.0,
                                    base=0, pattern=[[-1, P]], channel_multiplier=1).then_inc(ident_ready, 1)
            pool.wait_ge(consts_ready, 1)
            NB = BLOCKS_PER_BATCH
            pool_block(0, residuals=False)
            with pool.Fori(0, NB) as b:
                pool_block(b + 1)
            inverse_std(0, 0, 1)
            with pool.Fori(0, NB) as b:
                pool_block(b + NB + 1, norm0=True)
            inverse_std(1, 0, 2)
            with pool.Fori(2, BATCH - 1) as n:
                with pool.Fori(0, NB) as b:
                    pool_block(pool.snap(n * NB + b + 1), norm0=True, norm1=True)
                inverse_std(n, 0, 2)
            n = BATCH - 1
            with pool.Fori(n * NB + 1, BLOCKS - 1) as i:
                pool_block(i, norm0=True, norm1=True)
            pool_block(BLOCKS - 1, norm0=True, norm1=True)
            pool_block(BLOCKS, norm0=True, norm1=True)
            inverse_std(n, 0, 2)
            with pool.Fori(BLOCKS - NB, BLOCKS - 1) as i:
                add_residual(i)
            pool.wait_ge(act_norm1_done, NB)
            inverse_std(BATCH, 1, 2)


def kernel(**inputs):
    import numpy as np
    import concourse.bacc as bacc
    from concourse.bass_utils import run_bass_kernel_spmd

    nc = bacc.Bacc("TRN2", target_bir_lowering=False, num_devices=1)
    arrays = {}

    def dram_in(name, a):
        arrays[name] = np.ascontiguousarray(a)
        return nc.dram_tensor(name, a.shape, mybir.dt.from_np(a.dtype), kind="ExternalInput").ap()

    x = dram_in("x_dram", np.asarray(inputs["x"]))
    ctx_in = dram_in("ctx_dram", np.asarray(inputs["ctx_4096"]))
    mask = dram_in("mask_dram", np.asarray(inputs["mask_Bx1x4096_ff1"]))
    w_in_t, b_in, w_out_t, b_out = [], [], [], []
    for l in range(LAYERS):
        w_in_t.append(dram_in(f"w_in_t{l}_dram", np.asarray(inputs[f"L{l}_xattn_W_in"]).T))
        b_in.append(dram_in(f"b_in{l}_dram", np.asarray(inputs[f"L{l}_xattn_b_in"]).reshape(-1, P).T))
        w_out_t.append(dram_in(f"w_out_t{l}_dram", np.asarray(inputs[f"L{l}_xattn_W_out"]).T))
        b_out.append(dram_in(f"b_out{l}_dram", np.asarray(inputs[f"L{l}_xattn_b_out"]).reshape(-1, P).T))
    out = nc.dram_tensor("out_dram", (BATCH, CH, TIME), mybir.dt.float32, kind="ExternalOutput").ap()
    build_attention(nc, x, ctx_in, mask, w_in_t, b_in, w_out_t, b_out, out)
    r = run_bass_kernel_spmd(nc, [arrays], core_ids=[0])
    return r.results[0]["out_dram"]
```
